# Optimizing a Trainium2 kernel written in Bass

```python
import numpy as np
import jax
import jax.numpy as jnp

def _softmax(x, axis=-1):
    return jax.nn.softmax(x, axis=axis)

def _gelu(x):
    return jax.nn.gelu(x, approximate=True)

def _silu(x):
    return jax.nn.silu(x)

def _sigmoid(x):
    return jax.nn.sigmoid(x)

def _layernorm(x, axis=-1, eps=1e-05):
    m = jnp.mean(x, axis=axis, keepdims=True)
    v = jnp.var(x, axis=axis, keepdims=True)
    return (x - m) / jnp.sqrt(v + eps)

def _scatter_add(tgt, idx, src, axis=0):
    return tgt.at[idx].add(src)

def _segment_sum(src, seg, n):
    return jax.ops.segment_sum(src, seg, n)
kernel_name = 'mk_cond_resid_d2_seqx_r8_6e0e97'

def setup_inputs(seed: int=0):
    np.random.seed(seed)
    _w = jnp.asarray

    def _rec_inputs():
        import jax
        import jax.numpy as jnp
        _rk = jax.random.key(seed)
        x = -0.000125 + 0.9999 * jax.random.normal(jax.random.fold_in(_rk, 1), (32, 32, 128), jnp.float32)
        _lenS = 32 - jax.random.randint(jax.random.fold_in(_rk, 7), (32,), 0, max(1, 32 // 4) + 1, jnp.int32)
        _lenS2 = 32 - jax.random.randint(jax.random.fold_in(_rk, 8), (32,), 0, max(1, 32 // 4) + 1, jnp.int32)
        cond_1024 = -0.00493535 + 1.00056 * jax.random.normal(jax.random.fold_in(_rk, 11), (32, 128), jnp.float32)
        return (x, cond_1024)
    x, cond_1024 = _rec_inputs()

    def _L0_cond_setup():
        import jax, jax.numpy as jnp
        import numpy as np
        import math
        N, T, D, H = (64, 64, 128, 128)
        key = jax.random.key(seed)
        k1, k2, k3, k4 = jax.random.split(key, 4)
        x = jax.random.normal(k1, (N, T, D), dtype=jnp.float32)
        h0 = jax.random.normal(k2, (N, H), dtype=jnp.float32)
        Wx = jax.random.normal(k3, (D, 4 * H), dtype=jnp.float32) / math.sqrt(D)
        Wh = jax.random.normal(k4, (H, 4 * H), dtype=jnp.float32) / math.sqrt(H)
        b = jnp.zeros((4 * H,), dtype=jnp.float32)
        return {'x': x, 'h0': h0, 'Wx': Wx, 'Wh': Wh, 'b': b}
    _L0_cond_all = _L0_cond_setup()
    _L0_cond_in = {k: v for k, v in _L0_cond_all.items() if k in ('Wx', 'Wh', 'b')}
    del _L0_cond_all

    def _L1_cond_setup():
        import jax, jax.numpy as jnp
        import numpy as np
        B, T, D_IN, V_IN, E = (64, 128, 128, 128, 128)
        key = jax.random.key(seed)
        ks = jax.random.split(key, 16)
        s = 0.01
        return {'video': jax.random.normal(ks[0], (B, V_IN), jnp.float32), 'seq': jax.random.normal(ks[1], (B, T, D_IN), jnp.float32), 'W_z': jax.random.normal(ks[2], (D_IN, E), jnp.float32) * s, 'U_z': jax.random.normal(ks[3], (E, E), jnp.float32) * s, 'C_z': jax.random.normal(ks[4], (V_IN, E), jnp.float32) * s, 'b_z': jnp.zeros((E,), jnp.float32), 'W_r': jax.random.normal(ks[5], (D_IN, E), jnp.float32) * s, 'U_r': jax.random.normal(ks[6], (E, E), jnp.float32) * s, 'C_r': jax.random.normal(ks[7], (V_IN, E), jnp.float32) * s, 'b_r': jnp.zeros((E,), jnp.float32), 'W': jax.random.normal(ks[8], (D_IN, E), jnp.float32) * s, 'U': jax.random.normal(ks[9], (E, E), jnp.float32) * s, 'C': jax.random.normal(ks[10], (V_IN, E), jnp.float32) * s, 'b': jnp.zeros((E,), jnp.float32)}
    _L1_cond_all = _L1_cond_setup()
    _L1_cond_in = {k: v for k, v in _L1_cond_all.items() if k in ('W_z', 'U_z', 'C_z', 'b_z', 'W_r', 'U_r', 'C_r', 'b_r', 'W', 'U', 'C', 'b')}
    del _L1_cond_all
    return {'x': x, 'cond_1024': cond_1024, 'L0_cond_Wx': _L0_cond_in['Wx'], 'L0_cond_Wh': _L0_cond_in['Wh'], 'L0_cond_b': _L0_cond_in['b'], 'L1_cond_W_z': _L1_cond_in['W_z'], 'L1_cond_U_z': _L1_cond_in['U_z'], 'L1_cond_C_z': _L1_cond_in['C_z'], 'L1_cond_b_z': _L1_cond_in['b_z'], 'L1_cond_W_r': _L1_cond_in['W_r'], 'L1_cond_U_r': _L1_cond_in['U_r'], 'L1_cond_C_r': _L1_cond_in['C_r'], 'L1_cond_b_r': _L1_cond_in['b_r'], 'L1_cond_W': _L1_cond_in['W'], 'L1_cond_U': _L1_cond_in['U'], 'L1_cond_C': _L1_cond_in['C'], 'L1_cond_b': _L1_cond_in['b']}

def reference(x, cond_1024, L0_cond_Wx, L0_cond_Wh, L0_cond_b, L1_cond_W_z, L1_cond_U_z, L1_cond_C_z, L1_cond_b_z, L1_cond_W_r, L1_cond_U_r, L1_cond_C_r, L1_cond_b_r, L1_cond_W, L1_cond_U, L1_cond_C, L1_cond_b):
    import jax
    import jax.numpy as jnp

    def _L0_cond_ref(x, h0, Wx, Wh, b):
        import jax, jax.numpy as jnp
        import numpy as np
        import math
        N, T, D, H = (64, 64, 128, 128)
        Hdim = h0.shape[1]
        xW = jnp.einsum('ntd,dg->ntg', x, Wx) + b

        def step(carry, xw_t):
            prev_h, prev_c = carry
            a = xw_t + prev_h @ Wh
            i = jax.nn.sigmoid(a[:, :Hdim])
            f = jax.nn.sigmoid(a[:, Hdim:2 * Hdim])
            o = jax.nn.sigmoid(a[:, 2 * Hdim:3 * Hdim])
            g = jnp.tanh(a[:, 3 * Hdim:])
            next_c = f * prev_c + i * g
            next_h = o * jnp.tanh(next_c)
            return ((next_h, next_c), next_h)
        c0 = jnp.zeros_like(h0)
        _, hs = jax.lax.scan(step, (h0, c0), jnp.swapaxes(xW, 0, 1))
        return jnp.swapaxes(hs, 0, 1)

    def _L1_cond_ref(video, seq, W_z, U_z, C_z, b_z, W_r, U_r, C_r, b_r, W, U, C, b):
        import jax, jax.numpy as jnp
        import numpy as np
        B, T, D_IN, V_IN, E = (64, 128, 128, 128, 128)
        vz = video @ C_z + b_z
        vr = video @ C_r + b_r
        vh = video @ C + b
        xz = jnp.einsum('btd,de->bte', seq, W_z)
        xr = jnp.einsum('btd,de->bte', seq, W_r)
        xh = jnp.einsum('btd,de->bte', seq, W)

        def step(h, xs):
            xzt, xrt, xht = xs
            z = jax.nn.sigmoid(xzt + h @ U_z + vz)
            r = jax.nn.sigmoid(xrt + h @ U_r + vr)
            hh = jnp.tanh(xht + r * h @ U + vh)
            h_new = (1.0 - z) * h + z * hh
            return (h_new, h_new)
        h0 = jnp.zeros((seq.shape[0], U.shape[0]), seq.dtype)
        xs = (jnp.swapaxes(xz, 0, 1), jnp.swapaxes(xr, 0, 1), jnp.swapaxes(xh, 0, 1))
        _, out_t = jax.lax.scan(step, h0, xs)
        return jnp.swapaxes(out_t, 0, 1)
    x = x + _L0_cond_ref(x, cond_1024, L0_cond_Wx, L0_cond_Wh, L0_cond_b)
    x = x + _L1_cond_ref(cond_1024, x, L1_cond_W_z, L1_cond_U_z, L1_cond_C_z, L1_cond_b_z, L1_cond_W_r, L1_cond_U_r, L1_cond_C_r, L1_cond_b_r, L1_cond_W, L1_cond_U, L1_cond_C, L1_cond_b)
    return x

_drawn_inputs = setup_inputs


def setup_inputs(seed=0):
    import zlib

    import numpy as np

    out = dict(_drawn_inputs(seed))
    spreads = {'L0_cond_b': (0.0, 0.1),
     'L1_cond_b_z': (0.0, 2.0),
     'L1_cond_b_r': (0.0, 2.0),
     'L1_cond_b': (0.0, 0.1)}
    factors = {'L1_cond_W_z': 8.0,
     'L1_cond_U_z': 64.0,
     'L1_cond_C_z': 8.0,
     'L1_cond_W_r': 31.05,
     'L1_cond_U_r': 200.0,
     'L1_cond_C_r': 21.71,
     'L1_cond_U': 7.479}
    for name, (base, spread) in spreads.items():
        noise = np.random.default_rng([zlib.crc32(name.encode()), seed]).standard_normal(out[name].shape)
        drawn = base * np.exp(spread * noise) if base else spread * noise
        out[name] = jnp.asarray(drawn.astype(out[name].dtype))
    for name, factor in factors.items():
        out[name] = (out[name] * factor).astype(out[name].dtype)
    return out
```

```python
import concourse.bass as bass
from concourse import mybir
from contextlib import ExitStack

F32 = mybir.dt.float32
BF16 = mybir.dt.bfloat16
ALU = mybir.AluOpType
ACT = mybir.ActivationFunctionType


def lstm_then_gru_residual(nc, x, cond, Wx, Wh, b, W_z, U_z, C_z, b_z, W_r, U_r, C_r, b_r, W, U, C, b_h, out):
    N, T, D = x.shape
    P = 128
    assert D == P and Wx.shape[1] == 4 * P and T % 4 == 0 and 4 * N == P
    NG = 4
    L = NG * N
    R = 3 * N
    TG = P // N
    Q = T // TG
    NP = T // 2
    LAG = 3
    HEAD = 2

    x_groups = x.rearrange("b (q t) d -> q t b d", t=TG)
    out_groups = out.rearrange("b (q t) d -> q t b d", t=TG)

    ctx = ExitStack()
    with ctx:
        def sb(name, shape, dt=F32):
            return ctx.enter_context(nc.sbuf_tensor(name, shape, dt))

        def bank(name):
            return ctx.enter_context(nc.psum_tensor(name, [P, 512], F32))

        def sem(name):
            return ctx.enter_context(nc.semaphore(name))

        ident = sb("ident", [P, P])
        ident16 = sb("ident16", [P, P], BF16)
        x_rows = sb("x_rows", [P, Q, D])
        cond_rows = sb("cond_rows", [N, D])
        X2 = sb("X2", [P, T * N])
        condT = sb("condT", [P, N])
        Wx_raw = sb("Wx_raw", [P, NG * P])
        Wh_raw = sb("Wh_raw", [P, NG * P])
        Wx_s = sb("Wx_s", [P, NG * P])
        Wh_s = sb("Wh_s", [P, NG * P])
        gW_raw = sb("gW_raw", [P, 3, P])
        gU_raw = sb("gU_raw", [P, 3, P])
        gC = sb("gC", [P, 3, P])
        gW = sb("gW", [P, 3, P])
        gU = sb("gU", [P, 3, P])
        gb = sb("gb", [P, 3])
        V = sb("V", [P, 3, N])
        V_left = sb("V_left", [P, 2, R])
        V_part = sb("V_part", [P, 3, R], BF16)
        b_rows = sb("b_rows", [96, P])
        b_left = sb("b_left", [96, 2, P])
        b_part = sb("b_part", [96, 3, P], BF16)
        b_stat = sb("b_stat", [96, P], BF16)
        pick32 = sb("pick32", [96, NG])
        pick = sb("pick", [96, 2, NG, N], BF16)
        gates = sb("gates", [P, 2, 5 * N])
        vu = sb("vu", [P, 2, 2 * N])
        th = sb("th", [P, 2, N])
        H = sb("H", [P, 4 * N])
        X1 = sb("X1", [P, 4 * N])
        G = sb("G", [P, 4 * N])
        rz = sb("rz", [P, 2, 2 * N])
        hh = sb("hh", [P, 2, N])
        RH = sb("RH", [P, 2, N])
        An = sb("An", [P, 2, N])
        Pz = sb("Pz", [P, 2, N])
        Y = sb("Y", [P, 4 * N])
        y_rows = sb("y_rows", [P, D])
        warm = sb("warm", [P, 1])

        lstm_ps = [bank("lstm_ps0"), bank("lstm_ps1")]
        gru_ps = [bank("gru_ps0"), bank("gru_ps1")]
        xT_ps = [bank("xT_ps0"), bank("xT_ps1"), bank("xT_ps2")]
        XT_GROUPS = [(0, 1), (1, 4), (4, 8)]
        y_ps = bank("y_ps")
        cond_ps = y_ps

        x0_in = sem("x0_in")
        x_in = sem("x_in")
        cond_in = sem("cond_in")
        wx_in = sem("wx_in")
        wh_in = sem("wh_in")
        b_in = sem("b_in")
        gw_in = sem("gw_in")
        gu_in = sem("gu_in")
        gc_in = sem("gc_in")
        gb_in = sem("gb_in")
        ident_zero = sem("ident_zero")
        ident_ready = sem("ident_ready")
        ident16_ready = sem("ident16_ready")
        b_zero = sem("b_zero")
        pick_step = sem("pick_step")
        pick_ready = sem("pick_ready")
        xT_ready = sem("xT_ready")
        condT_ps_ready = sem("condT_ps_ready")
        x2_ready = sem("x2_ready")
        condT_ready = sem("condT_ready")
        wx_ready = sem("wx_ready")
        wh_ready = sem("wh_ready")
        b_step = sem("b_step")
        b_ready = sem("b_ready")
        gw_ready = sem("gw_ready")
        gu_ready = sem("gu_ready")
        v_ps_ready = sem("v_ps_ready")
        v_step = sem("v_step")
        v_ready = sem("v_ready")
        warm_zero = sem("warm_zero")
        c_ready = sem("c_ready")
        h_ready = sem("h_ready")
        g_ready = sem("g_ready")
        lstm_pre = sem("lstm_pre")
        gates_ready = sem("gates_ready")
        vu_ready = sem("vu_ready")
        th_ready = sem("th_ready")
        rz_pre = sem("rz_pre")
        rz_ready = sem("rz_ready")
        rh_ready = sem("rh_ready")
        hh_pre = sem("hh_pre")
        hh_ready = sem("hh_ready")
        an_ready = sem("an_ready")
        pz_ready = sem("pz_ready")
        x1_ready = sem("x1_ready")
        x1_used = sem("x1_used")
        y_ready = sem("y_ready")
        yT_ready = sem("yT_ready")
        y_rows_ready = sem("y_rows_ready")
        out_done = sem("out_done")

        block = ctx.enter_context(nc.Block())

        def lowest(k, s):
            return TG * k + s if isinstance(k, int) else TG * HEAD + s

        def highest(k, s):
            return TG * k + s if isinstance(k, int) else TG * (Q - 2) + s

        def run_slots(eng, slot):
            for k in range(HEAD):
                for s in range(TG):
                    slot(k, s)
            with eng.Fori(HEAD, Q - 1) as k:
                for s in range(TG):
                    slot(k, s)
            for s in range(TG + LAG):
                slot(Q - 1, s)

        @block.sync
        def _(sp):
            sp.dma_start(x_rows[:, 0, :], x_groups[0]).then_inc(x0_in, 16)
            sp.dma_start(Wh_raw[:, :], Wh).then_inc(wh_in, 16)
            for q in range(1, Q):
                sp.dma_start(x_rows[:, q, :], x_groups[q]).then_inc(x_in, 16)
            for g, w in enumerate((U_r, U_z, U)):
                sp.dma_start(gU_raw[:, g, :], w).then_inc(gu_in, 16)

            def store(q):
                sp.wait_ge(y_rows_ready, q + 1)
                sp.dma_start(out_groups[q], y_rows[:, :]).then_inc(out_done, 16)

            with sp.Fori(0, Q) as q:
                sp.wait_ge(y_rows_ready, q + 1)
                sp.dma_start(out_groups[bass.ds(q, 1)], y_rows[:, :]).then_inc(out_done, 16)
            sp.wait_ge(out_done, 16 * Q)

        @block.gpsimd
        def _(pool):
            nc.gpsimd.memset(ident[:, :], 0.0).then_inc(ident_zero, 1)
            pool.wait_ge(ident_zero, 1)
            nc.gpsimd.affine_select(out=ident[:, :], in_=ident[:, :], compare_op=ALU.not_equal, fill=1.0,
                                    base=0, pattern=[[-1, P]], channel_multiplier=1).then_inc(ident_ready, 1)
            nc.gpsimd.memset(pick32[:, :], 0.0).then_inc(pick_step, 1)
            for k in range(3):
                pool.wait_ge(pick_step, k + 1)
                nc.gpsimd.affine_select(out=pick32[:, :], in_=pick32[:, :], compare_op=ALU.not_equal,
                                        fill=1.0, base=-32 * k, pattern=[[-1, NG]],
                                        channel_multiplier=1).then_inc(pick_step, 1)
            pool.wait_ge(pick_step, 4)
            for j in range(2):
                for g in range(NG):
                    nc.gpsimd.tensor_scalar(pick[:, j, g, :], pick32[:, g:g + 1].to_broadcast([96, N]),
                                            0.5 if g < 3 else 1.0, None, ALU.mult).then_inc(pick_ready, 1)

            def slot(k, s):
                if s % 2 == 0 and 2 <= lowest(k, s) and highest(k, s) <= T:
                    p = 2 * k + s // 2 - 1
                    pool.wait_ge(h_ready, 2 * p + 3)
                    if lowest(k, s) == 2:
                        pool.wait_ge(x2_ready, 3)
                    if lowest(k, s) >= 4:
                        pool.wait_ge(x1_used, p - 1)
                        pool.wait_ge(y_ready, p - 1)
                    c = (s - 2) % 4 * N
                    nc.gpsimd.tensor_tensor(X1[:, c:c + 2 * N], X2[:, bass.ds(p * (2 * N), 2 * N)],
                                            H[:, c:c + 2 * N], ALU.add).then_inc(x1_ready, 1)
                if s % 2 == 0 and lowest(k, s) >= 4:
                    p = 2 * k + s // 2 - 2
                    pool.wait_ge(g_ready, 2 * p + 3)
                    if s == 0:
                        pool.wait_ge(yT_ready, k - 1)
                    if s == 4 and lowest(k, s) >= 8:
                        pool.wait_ge(yT_ready, k)
                    c = s % 4 * N
                    nc.gpsimd.tensor_tensor(Y[:, c:c + 2 * N], X1[:, c:c + 2 * N], G[:, c:c + 2 * N],
                                            ALU.add).then_inc(y_ready, 1)

            run_slots(pool, slot)

        @block.scalar
        def _(act):
            act.dma_start(cond_rows[:, :], cond).then_inc(cond_in, 16)
            act.dma_start(Wx_raw[:, :], Wx).then_inc(wx_in, 16)
            act.wait_ge(b_zero, 1)
            for k in range(3):
                act.dma_start(b_rows[32 * k:32 * k + NG, :], b.rearrange("(g d) -> g d", g=NG)).then_inc(b_in, 16)
            for g, w in enumerate((C_r, C_z, C)):
                act.dma_start(gC[:, g, :], w).then_inc(gc_in, 16)
            for g, w in enumerate((b_r, b_z, b_h)):
                act.dma_start(gb[:, g:g + 1], w.rearrange("(d a) -> d a", a=1)).then_inc(gb_in, 16)
            for g, w in enumerate((W_r, W_z, W)):
                act.dma_start(gW_raw[:, g, :], w).then_inc(gw_in, 16)
            act.wait_ge(warm_zero, 1)
            nc.scalar.activation(warm[:, :], warm[:, :], ACT.Tanh)
            act.wait_ge(condT_ps_ready, 1)
            nc.scalar.mul(H[:, 3 * N:4 * N], cond_ps[:, 0:N], 2.0).then_inc(h_ready, 1)
            nc.scalar.copy(condT[:, :], cond_ps[:, 0:N]).then_inc(condT_ready, 1)

            def x2_copy(i):
                a, e = XT_GROUPS[i]
                act.wait_ge(xT_ready, i + 1)
                nc.scalar.mul(X2[:, a * P:e * P], xT_ps[i][:, 0:(e - a) * P], 2.0).then_inc(x2_ready, 1)

            x2_copy(0)

            def slot(k, s):
                g = TG * k + s - LAG
                c, gs = s % 2, (s - LAG) % 4
                gru = lowest(k, s) >= LAG
                if gru:
                    act.wait_ge(rz_pre, g + 1)
                    nc.scalar.activation(rz[:, gs % 2, :],
                                         gru_ps[gs // 2][:, gs % 2 * R:gs % 2 * R + 2 * N],
                                         ACT.Tanh).then_inc(rz_ready, 1)
                if highest(k, s) < T:
                    t = TG * k + s
                    act.wait_ge(lstm_pre, t + 1)
                    nc.scalar.activation(gates[:, c, 0:L], lstm_ps[s // 2][:, c * L:(c + 1) * L],
                                         ACT.Tanh).then_inc(gates_ready, 1)
                if gru:
                    act.wait_ge(hh_pre, g + 1)
                    nc.scalar.activation(hh[:, gs % 2, :],
                                         gru_ps[gs // 2][:, gs % 2 * R + 2 * N:gs % 2 * R + 3 * N],
                                         ACT.Tanh).then_inc(hh_ready, 1)
                if highest(k, s) < T:
                    act.wait_ge(c_ready, t + 2)
                    nc.scalar.activation(th[:, c, :], gates[:, 1 - c, L:L + N], ACT.Tanh,
                                         scale=0.5).then_inc(th_ready, 1)
                if lowest(k, s) == highest(k, s) and lowest(k, s) in (0, 1):
                    x2_copy(s + 1)

            run_slots(act, slot)

        @block.vector
        def _(dve):
            nc.vector.memset(b_rows[:, :], 0.0).then_inc(b_zero, 1)
            nc.vector.memset(warm[:, :], 0.0).then_inc(warm_zero, 1)
            nc.vector.memset(gates[:, 0, L:L + N], 0.0).then_inc(c_ready, 1)
            nc.vector.memset(G[:, 3 * N:4 * N], 0.0).then_inc(g_ready, 1)
            dve.wait_ge(ident_ready, 1)
            nc.vector.tensor_copy(ident16[:, :], ident[:, :]).then_inc(ident16_ready, 1)

            def lstm_weights(dst, raw, arrived, ready):
                dve.wait_ge(arrived, 16)
                nc.vector.tensor_scalar(dst[:, 0:3 * P], raw[:, 0:3 * P], 0.25, None, ALU.mult).then_inc(ready, 1)
                nc.vector.tensor_scalar(dst[:, 3 * P:], raw[:, 3 * P:], 0.5, None, ALU.mult).then_inc(ready, 1)

            lstm_weights(Wx_s, Wx_raw, wx_in, wx_ready)
            lstm_weights(Wh_s, Wh_raw, wh_in, wh_ready)

            def split(whole, left, part, step, base):
                nc.vector.tensor_copy(part[:, 0, :], whole).then_inc(step, 1)
                dve.wait_ge(step, base + 1)
                nc.vector.tensor_tensor(left[:, 0, :], whole, part[:, 0, :], ALU.subtract).then_inc(step, 1)
                dve.wait_ge(step, base + 2)
                nc.vector.tensor_copy(part[:, 1, :], left[:, 0, :]).then_inc(step, 1)
                dve.wait_ge(step, base + 3)
                nc.vector.tensor_tensor(left[:, 1, :], left[:, 0, :], part[:, 1, :], ALU.subtract).then_inc(step, 1)
                dve.wait_ge(step, base + 4)
                nc.vector.tensor_copy(part[:, 2, :], left[:, 1, :]).then_inc(step, 1)
                dve.wait_ge(step, base + 5)

            dve.wait_ge(b_in, 48)
            split(b_rows[:, :], b_left, b_part, b_step, 0)
            for k in range(3):
                nc.vector.tensor_copy(b_stat[32 * k:32 * k + 32, :],
                                      b_part[32 * k:32 * k + 32, k, :]).then_inc(b_ready, 1)

            def v_setup():
                dve.wait_ge(gb_in, 48)
                dve.wait_ge(v_ps_ready, 1)
                for g in range(3):
                    nc.vector.tensor_scalar(V[:, g, :], cond_ps[:, 128 + g * N:128 + (g + 1) * N],
                                            gb[:, g:g + 1], 0.5 if g < 2 else 1.0,
                                            ALU.add, ALU.mult).then_inc(v_step, 1)
                dve.wait_ge(v_step, 3)
                split(V[:, :, :].rearrange("p g n -> p (g n)"), V_left, V_part, v_step, 3)
                nc.vector.tensor_copy(V_left[:, 0, 0:1], V_left[:, 1, 0:1]).then_inc(v_ready, 1)

            def gru_weights():
                dve.wait_ge(gw_in, 48)
                nc.vector.tensor_scalar(gW[:, 0:2, :], gW_raw[:, 0:2, :], 0.25, None, ALU.mult).then_inc(gw_ready, 1)
                nc.vector.tensor_scalar(gW[:, 2, :], gW_raw[:, 2, :], 0.5, None, ALU.mult).then_inc(gw_ready, 1)
                dve.wait_ge(gu_in, 48)
                nc.vector.tensor_scalar(gU[:, :, :], gU_raw[:, :, :], 0.25, None, ALU.mult).then_inc(gu_ready, 1)

            def slot(k, s):
                g = TG * k + s - LAG
                c, gs = s % 2, (s - LAG) % 4
                gc = gs * N
                gprev = (gs - 1) % 4 * N
                gru = lowest(k, s) >= LAG
                lstm = highest(k, s) < T
                if gru:
                    dve.wait_ge(rz_ready, g + 1)
                    dve.wait_ge(g_ready, g + 1)
                    nc.vector.scalar_tensor_tensor(out=RH[:, gs % 2, :], in0=rz[:, gs % 2, 0:N], scalar=1.0,
                                                   in1=G[:, gprev:gprev + N], op0=ALU.add,
                                                   op1=ALU.mult).then_inc(rh_ready, 1)
                    nc.vector.scalar_tensor_tensor(out=An[:, gs % 2, :], in0=rz[:, gs % 2, N:2 * N], scalar=-1.0,
                                                   in1=G[:, gprev:gprev + N], op0=ALU.add,
                                                   op1=ALU.mult).then_inc(an_ready, 1)
                if lstm:
                    t = TG * k + s
                    dve.wait_ge(gates_ready, t + 1)
                    dve.wait_ge(c_ready, t + 1)
                    nc.vector.scalar_tensor_tensor(out=vu[:, c, :], in0=gates[:, c, 0:2 * N], scalar=1.0,
                                                   in1=gates[:, c, 3 * N:5 * N], op0=ALU.add,
                                                   op1=ALU.mult).then_inc(vu_ready, 1)
                    dve.wait_ge(vu_ready, t + 1)
                    nc.vector.scalar_tensor_tensor(out=gates[:, 1 - c, L:L + N], in0=vu[:, c, N:2 * N], scalar=0.5,
                                                   in1=vu[:, c, 0:N], op0=ALU.mult,
                                                   op1=ALU.add).then_inc(c_ready, 1)
                if gru:
                    dve.wait_ge(hh_ready, g + 1)
                    nc.vector.scalar_tensor_tensor(out=Pz[:, gs % 2, :], in0=rz[:, gs % 2, N:2 * N], scalar=1.0,
                                                   in1=hh[:, gs % 2, :], op0=ALU.add,
                                                   op1=ALU.mult).then_inc(pz_ready, 1)
                    dve.wait_ge(an_ready, g + 1)
                    dve.wait_ge(pz_ready, g + 1)
                    nc.vector.scalar_tensor_tensor(out=G[:, gc:gc + N], in0=An[:, gs % 2, :], scalar=-0.5,
                                                   in1=Pz[:, gs % 2, :], op0=ALU.mult,
                                                   op1=ALU.add).then_inc(g_ready, 1)
                if lstm:
                    dve.wait_ge(th_ready, t + 1)
                    nc.vector.scalar_tensor_tensor(out=H[:, s % 4 * N:(s % 4 + 1) * N], in0=gates[:, c, 2 * N:3 * N],
                                                   scalar=1.0, in1=th[:, c, :], op0=ALU.add,
                                                   op1=ALU.mult).then_inc(h_ready, 1)
                if lowest(k, s) == 0:
                    v_setup()
                    gru_weights()
                if s == 3 and lowest(k, s) >= 7:
                    y_out(k - 1)

            def y_out(q):
                dve.wait_ge(yT_ready, q + 1)
                if not isinstance(q, int) or q >= 1:
                    dve.wait_ge(out_done, 16 * q)
                nc.vector.tensor_scalar(y_rows[:, :], y_ps[:, 0:P], 0.5, None, ALU.mult).then_inc(y_rows_ready, 1)

            run_slots(dve, slot)
            y_out(Q - 1)

        @block.tensor
        def _(pe):
            def mm(out_, lhsT, rhs, start=False):
                return nc.tensor.matmul(out_, lhsT, rhs, start=start, stop=False, skip_group_check=True)

            def x_transpose(i):
                a, e = XT_GROUPS[i]
                pe.wait_ge(x0_in if i == 0 else x_in, 16 if i == 0 else 16 * (Q - 1))
                for q in range(a, e):
                    last = nc.tensor.transpose(xT_ps[i][:, (q - a) * P:(q - a + 1) * P], x_rows[:, q, :], ident[:, :])
                last.then_inc(xT_ready, 1)

            def pair_cols(ps, width, g):
                return ps[:, 0:2 * width].rearrange("p (j w) -> p j w", j=2)[:, :, g * N:(g + 1) * N]

            def lstm_bias(p, b_):
                mm(lstm_ps[b_][:, 0:2 * L], b_stat[:, :], pick[:, :, :, :].rearrange("p j g n -> p (j g n)"), start=True)

            def lstm_x(p, b_, gs):
                for g in gs:
                    mm(pair_cols(lstm_ps[b_], L, g), Wx_s[:, g * P:(g + 1) * P], X2[:, bass.ds(p * (2 * N), 2 * N)])

            def gru_const(b_):
                for k in range(3):
                    mm(gru_ps[b_][:, 0:2 * R], ident16[:, :], V_part[:, k:k + 1, :].to_broadcast([P, 2, R]),
                       start=(k == 0))

            pe.wait_ge(ident_ready, 1)
            pe.wait_ge(cond_in, 16)
            nc.tensor.transpose(cond_ps[:, 0:N], cond_rows[:, :], ident[0:N, 0:N]).then_inc(condT_ps_ready, 1)
            x_transpose(0)
            pe.wait_ge(b_ready, 3)
            pe.wait_ge(pick_ready, 2 * NG)
            lstm_bias(0, 0)
            pe.wait_ge(wx_ready, 2)
            pe.wait_ge(x2_ready, 1)
            lstm_x(0, 0, range(NG))
            pe.wait_ge(wh_ready, 2)

            def slot(k, s):
                t = TG * k + s
                c, gs = s % 2, (s - LAG) % 4
                if highest(k, s) < T:
                    pe.wait_ge(h_ready, t + 1)
                    hp = (s - 1) % 4 * N
                    for g in range(NG):
                        last = mm(lstm_ps[s // 2][:, c * L + g * N:c * L + (g + 1) * N],
                                  Wh_s[:, g * P:(g + 1) * P], H[:, hp:hp + N])
                    last.then_inc(lstm_pre, 1)
                if lowest(k, s) == 0:
                    pe.wait_ge(gc_in, 48)
                    pe.wait_ge(condT_ready, 1)
                    for g in range(3):
                        last = nc.tensor.matmul(cond_ps[:, 128 + g * N:128 + (g + 1) * N], gC[:, g, :], condT[:, :],
                                                start=(g == 0), stop=True, skip_group_check=True)
                    last.then_inc(v_ps_ready, 1)
                    x_transpose(1)
                if lowest(k, s) == 1:
                    x_transpose(2)
                if lowest(k, s) >= LAG:
                    pe.wait_ge(rh_ready, t - LAG + 1)
                    mm(gru_ps[gs // 2][:, gs % 2 * R + 2 * N:gs % 2 * R + 3 * N], gU[:, 2, :],
                       RH[:, gs % 2, :]).then_inc(hh_pre, 1)
                if highest(k, s) < T - 2:
                    p = 2 * k + s // 2 + 1
                    if lowest(k, s) == 2:
                        pe.wait_ge(x2_ready, 3)
                    if s % 2 == 0:
                        if lowest(k, s) >= 2:
                            pe.wait_ge(gates_ready, t)
                        lstm_bias(p, (s // 2 + 1) % 2)
                        lstm_x(p, (s // 2 + 1) % 2, [0])
                    else:
                        lstm_x(p, (s // 2 + 1) % 2, [1, 2, 3])
                if s % 2 == 1 and highest(k, s) < T:
                    if lowest(k, s) == 1:
                        pe.wait_ge(ident16_ready, 1)
                        pe.wait_ge(v_ready, 1)
                    if lowest(k, s) >= 5:
                        pe.wait_ge(hh_ready, t - 3)
                    gru_const(s // 2 % 2)
                if s % 2 == 0 and 2 <= lowest(k, s) and highest(k, s) <= T:
                    p = 2 * k + s // 2 - 1
                    if lowest(k, s) == 2:
                        pe.wait_ge(gw_ready, 2)
                        pe.wait_ge(gu_ready, 1)
                    pe.wait_ge(x1_ready, p + 1)
                    a = (s - 2) % 4 * N
                    for g in range(3):
                        last = mm(pair_cols(gru_ps[(s // 2 - 1) % 2], R, g), gW[:, g, :], X1[:, a:a + 2 * N])
                    last.then_inc(x1_used, 1)
                if s == 3 and lowest(k, s) >= 7:
                    y_transpose(k - 1)
                if lowest(k, s) >= 2 and highest(k, s) < T + 2:
                    g2 = (s - 2) % 4
                    pe.wait_ge(g_ready, t - 1)
                    gp = (g2 - 1) % 4 * N
                    for g in range(2):
                        last = mm(gru_ps[g2 // 2][:, g2 % 2 * R + g * N:g2 % 2 * R + (g + 1) * N], gU[:, g, :],
                                  G[:, gp:gp + N])
                    last.then_inc(rz_pre, 1)

            def y_transpose(q):
                pe.wait_ge(y_ready, 2 * q + 2)
                if not isinstance(q, int) or q >= 1:
                    pe.wait_ge(y_rows_ready, q)
                nc.tensor.transpose(y_ps[:, 0:P], Y[:, :], ident[:, :]).then_inc(yT_ready, 1)

            run_slots(pe, slot)
            y_transpose(Q - 1)


_INS = ['x', 'cond_1024', 'L0_cond_Wx', 'L0_cond_Wh', 'L0_cond_b',
        'L1_cond_W_z', 'L1_cond_U_z', 'L1_cond_C_z', 'L1_cond_b_z',
        'L1_cond_W_r', 'L1_cond_U_r', 'L1_cond_C_r', 'L1_cond_b_r',
        'L1_cond_W', 'L1_cond_U', 'L1_cond_C', 'L1_cond_b']


def kernel(**inputs):
    import numpy as _np
    import concourse.bacc as _bacc
    from concourse import mybir as _mybir
    from concourse.bass_utils import run_bass_kernel_spmd as _run

    nc = _bacc.Bacc("TRN2", target_bir_lowering=False, num_devices=1)
    arrays, args = {}, []
    for name in _INS:
        a = _np.ascontiguousarray(inputs[name])
        arrays[f"in_{name}_dram"] = a
        args.append(nc.dram_tensor(f"in_{name}_dram", a.shape, _mybir.dt.from_np(a.dtype), kind="ExternalInput").ap())
    args.append(nc.dram_tensor("out_0_dram", inputs["x"].shape, _mybir.dt.float32, kind="ExternalOutput").ap())
    lstm_then_gru_residual(nc, *args)
    r = _run(nc, [arrays], core_ids=[0])
    return r.results[0]["out_0_dram"]
```

```python
import concourse.bass as bass
from concourse import mybir
from contextlib import ExitStack

F32 = mybir.dt.float32
BF16 = mybir.dt.bfloat16
F16 = mybir.dt.float16
ALU = mybir.AluOpType
ACT = mybir.ActivationFunctionType


def lstm_then_gru_residual(nc, x, cond, Wx, Wh, b, W_z, U_z, C_z, b_z, W_r, U_r, C_r, b_r, W, U, C, b_h, out):
    N, T, D = x.shape
    P = 128
    assert D == P and Wx.shape[1] == 4 * P and T % 4 == 0 and 4 * N == P
    NG = 4
    L = NG * N
    TG = P // N
    Q = T // TG
    NP = T // 2
    LAG = 3
    BUSY = 8

    x_groups = x.rearrange("b (q t) d -> q t b d", t=TG)
    out_groups = out.rearrange("b (q t) d -> q t b d", t=TG)

    ctx = ExitStack()
    with ctx:
        def sb(name, shape, dt=F32):
            return ctx.enter_context(nc.sbuf_tensor(name, shape, dt))

        def bank(name):
            return ctx.enter_context(nc.psum_tensor(name, [P, 512], F32))

        def sem(name):
            return ctx.enter_context(nc.semaphore(name))

        ident = sb("ident", [P, P])
        x_rows = sb("x_rows", [P, Q, D])
        cond_rows = sb("cond_rows", [N, D])
        X2 = sb("X2", [P, T * N])
        condT = sb("condT", [P, N])
        Wx_raw = sb("Wx_raw", [P, NG * P])
        Wh_raw = sb("Wh_raw", [P, NG * P])
        Wx_s = sb("Wx_s", [P, NG * P])
        condT_half = sb("condT_half", [P, N])
        Wh_part = sb("Wh_part", [P, 3, NG * P], BF16)
        Wh_left = sb("Wh_left", [P, 1, NG * P])
        gW_raw = sb("gW_raw", [P, 3, P])
        gU_raw = sb("gU_raw", [P, 3, P])
        gC = sb("gC", [P, 3, P])
        gW = sb("gW", [P, 3, P])
        gU = sb("gU", [P, 3, P])
        gb = sb("gb", [P, 3])
        V_rh = sb("V_rh", [P, 2, 2, N])
        V_z = sb("V_z", [P, 2, N])
        b_cols = sb("b_cols", [P, NG])
        b_wide = sb("b_wide", [P, TG, NG, N])
        gates = sb("gates", [P, 2, 5 * N])
        vu = sb("vu", [P, 2, 2 * N])
        th = sb("th", [P, 2, N])
        H = sb("H", [P, 4 * N])
        H_part = sb("H_part", [P, 2, 2, N], F16)
        X1 = sb("X1", [P, 4 * N])
        G = sb("G", [P, 4 * N])
        tr = sb("tr", [P, 2, N])
        tz = sb("tz", [P, 2, N])
        hh = sb("hh", [P, 2, N])
        RH = sb("RH", [P, 2, N])
        An = sb("An", [P, 2, N])
        Pz = sb("Pz", [P, 2, N])
        Y = sb("Y", [P, 4 * N])
        y_rows = sb("y_rows", [P, D])
        warm = sb("warm", [P, 1])
        busy = sb("busy", [P, P], BF16)

        lstm_ps = [bank("lstm_ps0"), bank("lstm_ps1")]
        rh_ps = [bank("rh_ps0"), bank("rh_ps1")]
        z_ps = [bank("z_ps0"), bank("z_ps1")]
        xT_ps = [rh_ps[0], z_ps[0], z_ps[1]]
        idle_ps = bank("idle_ps")
        XT_GROUPS = [(0, 1), (1, 4), (4, 8)]
        y_ps = bank("y_ps")
        cond_ps = y_ps

        x0_in = sem("x0_in")
        x_in = sem("x_in")
        cond_in = sem("cond_in")
        wx_in = sem("wx_in")
        wh_in = sem("wh_in")
        b_in = sem("b_in")
        gw_in = sem("gw_in")
        gu_in = sem("gu_in")
        gc_in = sem("gc_in")
        gb_in = sem("gb_in")
        ident_zero = sem("ident_zero")
        ident_ready = sem("ident_ready")
        opened = sem("opened")
        xT_ready = sem("xT_ready")
        condT_ps_ready = sem("condT_ps_ready")
        x2_ready = sem("x2_ready")
        condT_ready = sem("condT_ready")
        wx_ready = sem("wx_ready")
        wh_step = sem("wh_step")
        wh_left_ready = sem("wh_left_ready")
        wh_ready = sem("wh_ready")
        b_ready = sem("b_ready")
        gw_ready = sem("gw_ready")
        gu_ready = sem("gu_ready")
        v_ps_ready = sem("v_ps_ready")
        v_ready = sem("v_ready")
        lstm_seeded = sem("lstm_seeded")
        gru_seeded = sem("gru_seeded")
        warm_zero = sem("warm_zero")
        busy_zero = sem("busy_zero")
        c_ready = sem("c_ready")
        h_hi_ready = sem("h_hi_ready")
        h_ready = sem("h_ready")
        h_lo_ready = sem("h_lo_ready")
        g_ready = sem("g_ready")
        lstm_pre = sem("lstm_pre")
        gates_ready = sem("gates_ready")
        vu_ready = sem("vu_ready")
        th_ready = sem("th_ready")
        r_pre = sem("r_pre")
        z_pre = sem("z_pre")
        r_ready = sem("r_ready")
        z_ready = sem("z_ready")
        rh_ready = sem("rh_ready")
        hh_pre = sem("hh_pre")
        hh_ready = sem("hh_ready")
        pz_ready = sem("pz_ready")
        x1_ready = sem("x1_ready")
        x1_used = sem("x1_used")
        y_ready = sem("y_ready")
        yT_ready = sem("yT_ready")
        y_rows_ready = sem("y_rows_ready")
        out_done = sem("out_done")

        block = ctx.enter_context(nc.Block())

        def r_cols(g):
            return rh_ps[g // 2 % 2][:, g % 2 * 2 * N:g % 2 * 2 * N + N]

        def hh_cols(g):
            return rh_ps[g // 2 % 2][:, g % 2 * 2 * N + N:g % 2 * 2 * N + 2 * N]

        def z_cols(g):
            return z_ps[g // 2 % 2][:, g % 2 * N:g % 2 * N + N]

        def run_slots(slot):
            for t in range(T + LAG):
                slot(t)

        @block.sync
        def _(sp):
            sp.dma_start(x_rows[:, 0, :], x_groups[0]).then_inc(x0_in, 16)
            sp.dma_start(b_cols[:, :], b.rearrange("(g d) -> d g", g=NG), allow_slow_non_contiguous=True).then_inc(b_in, 16)
            sp.dma_start(Wh_raw[:, :], Wh).then_inc(wh_in, 16)
            for j in range(TG):
                sp.dma_start(x_rows[j * N:(j + 1) * N, 1:Q, :],
                             x.rearrange("b (q t) d -> t b q d", t=TG)[j, :, 1:Q, :]).then_inc(x_in, 16)
            for j, w in enumerate((C_r, C_z, C)):
                sp.dma_start(gC[:, j, :], w).then_inc(gc_in, 16)
            for j, w in enumerate((b_r, b_z, b_h)):
                sp.dma_start(gb[:, j:j + 1], w.rearrange("(d a) -> d a", a=1)).then_inc(gb_in, 16)
            for j, w in enumerate((W_r, W_z, W)):
                sp.dma_start(gW_raw[:, j, :], w).then_inc(gw_in, 16)
            for j, w in enumerate((U_r, U_z, U)):
                sp.dma_start(gU_raw[:, j, :], w).then_inc(gu_in, 16)

            with sp.Fori(0, Q) as q:
                sp.wait_ge(y_rows_ready, q + 1)
                sp.dma_start(out_groups[bass.ds(q, 1)], y_rows[:, :]).then_inc(out_done, 16)
            sp.wait_ge(out_done, 16 * Q)

        @block.gpsimd
        def _(pool):
            nc.gpsimd.memset(ident[:, :], 0.0).then_inc(ident_zero, 1)
            pool.wait_ge(ident_zero, 1)
            nc.gpsimd.affine_select(out=ident[:, :], in_=ident[:, :], compare_op=ALU.not_equal, fill=1.0,
                                    base=0, pattern=[[-1, P]], channel_multiplier=1).then_inc(ident_ready, 1)
            def slot(t):
                if t % 2 == 0 and 2 <= t <= T:
                    p = t // 2 - 1
                    pool.wait_ge(h_ready, 2 * p + 2)
                    if p in (0, 2, 8):
                        pool.wait_ge(x2_ready, 1 + (p > 0) + (p > 2))
                    if p >= 2:
                        pool.wait_ge(x1_used, p - 1)
                        pool.wait_ge(y_ready, p - 1)
                    c = 2 * p % 4 * N
                    nc.gpsimd.tensor_tensor(X1[:, c:c + 2 * N], X2[:, p * 2 * N:(p + 1) * 2 * N],
                                            H[:, c:c + 2 * N], ALU.add).then_inc(x1_ready, 1)
                if t % 2 == 0 and t >= 4:
                    p = t // 2 - 2
                    pool.wait_ge(g_ready, 2 * p + 3)
                    if p % 2 == 0 and p >= 2:
                        pool.wait_ge(yT_ready, p // 2)
                    c = 2 * p % 4 * N
                    nc.gpsimd.tensor_tensor(Y[:, c:c + 2 * N], X1[:, c:c + 2 * N], G[:, c:c + 2 * N],
                                            ALU.add).then_inc(y_ready, 1)

            run_slots(slot)

        @block.scalar
        def _(act):
            act.dma_start(Wx_raw[:, :], Wx).then_inc(wx_in, 16)
            act.dma_start(cond_rows[:, :], cond).then_inc(cond_in, 16)
            act.wait_ge(warm_zero, 1)
            nc.scalar.activation(warm[:, :], warm[:, :], ACT.Tanh)
            def seed_lstm(k):
                nc.scalar.copy(lstm_ps[k % 2][:, :], b_wide[:, :, :, :].rearrange("p t g n -> p (t g n)")
                               ).then_inc(lstm_seeded, 1)

            def seed_gru(p):
                nc.scalar.copy(rh_ps[p % 2][:, 0:4 * N], V_rh[:, :, :, :].rearrange("p t g n -> p (t g n)")
                               ).then_inc(gru_seeded, 1)
                nc.scalar.copy(z_ps[p % 2][:, 0:2 * N], V_z[:, :, :].rearrange("p t n -> p (t n)")
                               ).then_inc(gru_seeded, 1)

            act.wait_ge(b_ready, NG)
            act.wait_ge(opened, 2)
            seed_lstm(0)
            act.wait_ge(condT_ps_ready, 1)
            nc.scalar.mul(condT_half[:, :], cond_ps[:, 0:N], 0.5).then_inc(condT_ready, 1)
            nc.scalar.copy(condT[:, :], cond_ps[:, 0:N]).then_inc(condT_ready, 1)

            def x2_copy(i):
                a, e = XT_GROUPS[i]
                act.wait_ge(xT_ready, i + 1)
                nc.scalar.mul(X2[:, a * P:e * P], xT_ps[i][:, 0:(e - a) * P], 2.0).then_inc(x2_ready, 1)

            x2_copy(0)

            def wh_part(k, src, scale_ifo, scale_g):
                nc.scalar.mul(Wh_part[:, k, 0:3 * P], src[:, 0:3 * P], scale_ifo).then_inc(wh_step, 1)
                nc.scalar.mul(Wh_part[:, k, 3 * P:], src[:, 3 * P:], scale_g).then_inc(wh_step, 1)

            act.wait_ge(wh_in, 16)
            wh_part(0, Wh_raw, 0.25, 0.5)
            act.wait_ge(wh_left_ready, 2)
            wh_part(1, Wh_left[:, 0, :], 1.0, 1.0)

            def slot(t):
                g = t - LAG
                if t < T:
                    act.wait_ge(lstm_pre, t + 1)
                    nc.scalar.activation(gates[:, t % 2, 0:L], lstm_ps[t // TG % 2][:, t % TG * L:(t % TG + 1) * L],
                                         ACT.Tanh).then_inc(gates_ready, 1)
                if g >= 0:
                    act.wait_ge(r_pre, g + 1)
                    nc.scalar.activation(tr[:, g % 2, :], r_cols(g), ACT.Tanh).then_inc(r_ready, 1)
                    act.wait_ge(z_pre, g + 1)
                    nc.scalar.activation(tz[:, g % 2, :], z_cols(g), ACT.Tanh).then_inc(z_ready, 1)
                if t < T:
                    act.wait_ge(c_ready, t + 2)
                    nc.scalar.activation(th[:, t % 2, :], gates[:, (t + 1) % 2, L:L + N], ACT.Tanh,
                                         scale=0.5).then_inc(th_ready, 1)
                if g >= 0:
                    act.wait_ge(hh_pre, g + 1)
                    nc.scalar.activation(hh[:, g % 2, :], hh_cols(g), ACT.Tanh).then_inc(hh_ready, 1)
                if t < 2:
                    x2_copy(t + 1)
                if t == 0:
                    seed_lstm(1)
                if t == 1:
                    act.wait_ge(gw_in, 48)
                    nc.scalar.mul(gW[:, 0:2, :], gW_raw[:, 0:2, :], 0.25).then_inc(gw_ready, 1)
                    nc.scalar.mul(gW[:, 2, :], gW_raw[:, 2, :], 0.5).then_inc(gw_ready, 1)
                    act.wait_ge(v_ready, 3)
                    act.wait_ge(opened, 5)
                    seed_gru(0)
                if t == 2:
                    act.wait_ge(opened, 6)
                if t % 2 == 0 and 2 <= t < T:
                    if t >= 4:
                        act.wait_ge(hh_ready, t - 2)
                    seed_gru(t // 2)
                if t % TG == TG - 1 and t // TG + 2 < Q:
                    act.wait_ge(gates_ready, t + 1)
                    seed_lstm(t // TG + 2)

            run_slots(slot)

        @block.vector
        def _(dve):
            nc.vector.memset(busy[:, :], 0.0).then_inc(busy_zero, 1)
            nc.vector.memset(warm[:, :], 0.0).then_inc(warm_zero, 1)
            nc.vector.memset(gates[:, 0, L:L + N], 0.0).then_inc(c_ready, 1)
            nc.vector.memset(G[:, 3 * N:4 * N], 0.0).then_inc(g_ready, 1)

            def lstm_weights(dst, raw, arrived, ready):
                dve.wait_ge(arrived, 16)
                nc.vector.tensor_scalar(dst[:, 0:3 * P], raw[:, 0:3 * P], 0.25, None, ALU.mult).then_inc(ready, 1)
                nc.vector.tensor_scalar(dst[:, 3 * P:], raw[:, 3 * P:], 0.5, None, ALU.mult).then_inc(ready, 1)

            dve.wait_ge(b_in, 16)
            for g in range(NG):
                nc.vector.tensor_scalar(b_wide[:, :, g, :], b_cols[:, g:g + 1].rearrange("p (a b) -> p a b", a=1)
                                        .to_broadcast([P, TG, N]), 0.5 if g < 3 else 1.0, None,
                                        ALU.mult).then_inc(b_ready, 1)
            lstm_weights(Wx_s, Wx_raw, wx_in, wx_ready)

            def wh_split():
                dve.wait_ge(wh_step, 2)
                for c, e, f in ((0, 3 * P, 0.25), (3 * P, 4 * P, 0.5)):
                    nc.vector.scalar_tensor_tensor(out=Wh_left[:, 0, c:e], in0=Wh_raw[:, c:e], scalar=f,
                                                   in1=Wh_part[:, 0, c:e], op0=ALU.mult,
                                                   op1=ALU.subtract).then_inc(wh_left_ready, 1)
                dve.wait_ge(wh_step, 4)
                nc.vector.tensor_tensor(Wh_part[:, 2, :], Wh_left[:, 0, :], Wh_part[:, 1, :],
                                        ALU.subtract).then_inc(wh_ready, 1)

            wh_split()

            def v_setup():
                dve.wait_ge(gb_in, 48)
                dve.wait_ge(v_ps_ready, 1)
                for g, dst in enumerate((V_rh[:, :, 0, :], V_z[:, :, :], V_rh[:, :, 1, :])):
                    nc.vector.tensor_scalar(dst, cond_ps[:, 128 + g * N:128 + (g + 1) * N]
                                            .rearrange("p (a n) -> p a n", a=1).to_broadcast([P, 2, N]),
                                            gb[:, g:g + 1], 0.5 if g < 2 else 1.0,
                                            ALU.add, ALU.mult).then_inc(v_ready, 1)

            def stt(out_, in0, scalar, in1, op0, op1):
                return nc.vector.scalar_tensor_tensor(out=out_, in0=in0, scalar=scalar, in1=in1, op0=op0, op1=op1)

            def slot(t):
                g = t - LAG
                b_, gb_ = t % 2, g % 2
                hc, gc, gp = t % 4 * N, g % 4 * N, (g - 1) % 4 * N
                if t < T:
                    if t == 0:
                        dve.wait_ge(c_ready, 1)
                    dve.wait_ge(gates_ready, t + 1)
                    stt(vu[:, b_, :], gates[:, b_, 0:2 * N], 1.0, gates[:, b_, 3 * N:5 * N],
                        ALU.add, ALU.mult).then_inc(vu_ready, 1)
                if g >= 0:
                    dve.wait_ge(r_ready, g + 1)
                    stt(RH[:, gb_, :], tr[:, gb_, :], 1.0, G[:, gp:gp + N], ALU.add, ALU.mult).then_inc(rh_ready, 1)
                if t < T:
                    dve.wait_ge(vu_ready, t + 1)
                    stt(gates[:, 1 - b_, L:L + N], vu[:, b_, N:2 * N], 0.5, vu[:, b_, 0:N],
                        ALU.mult, ALU.add).then_inc(c_ready, 1)
                if g >= 0:
                    dve.wait_ge(z_ready, g + 1)
                    stt(An[:, gb_, :], tz[:, gb_, :], -1.0, G[:, gp:gp + N], ALU.add, ALU.mult)
                if t < T:
                    dve.wait_ge(th_ready, t + 1)
                    stt(H_part[:, b_, 0, :], gates[:, b_, 2 * N:3 * N], 1.0, th[:, b_, :],
                        ALU.add, ALU.mult).then_inc(h_hi_ready, 1)
                    stt(H[:, hc:hc + N], gates[:, b_, 2 * N:3 * N], 1.0, th[:, b_, :],
                        ALU.add, ALU.mult).then_inc(h_ready, 1)
                if g >= 0:
                    dve.wait_ge(hh_ready, g + 1)
                    stt(Pz[:, gb_, :], tz[:, gb_, :], 1.0, hh[:, gb_, :], ALU.add, ALU.mult).then_inc(pz_ready, 1)
                if t < T - 1:
                    dve.wait_ge(h_ready, t + 1)
                    nc.vector.tensor_tensor(H_part[:, b_, 1, :], H[:, hc:hc + N], H_part[:, b_, 0, :],
                                            ALU.subtract).then_inc(h_lo_ready, 1)
                if g >= 0:
                    dve.wait_ge(pz_ready, g + 1)
                    stt(G[:, gc:gc + N], An[:, gb_, :], -0.5, Pz[:, gb_, :], ALU.mult, ALU.add).then_inc(g_ready, 1)
                if t == 0:
                    v_setup()
                if t == 1:
                    dve.wait_ge(gu_in, 48)
                    nc.vector.tensor_scalar(gU[:, :, :], gU_raw[:, :, :], 0.25, None, ALU.mult).then_inc(gu_ready, 1)
                if t % TG == 3 and t >= 7:
                    y_out(t // TG - 1)

            def y_out(q):
                dve.wait_ge(yT_ready, q + 1)
                if q >= 1:
                    dve.wait_ge(out_done, 16 * q)
                nc.vector.tensor_scalar(y_rows[:, :], y_ps[:, 0:P], 0.5, None, ALU.mult).then_inc(y_rows_ready, 1)

            run_slots(slot)
            y_out(Q - 1)

        @block.tensor
        def _(pe):
            def mm(out_, lhsT, rhs):
                return nc.tensor.matmul(out_, lhsT, rhs, start=False, stop=False, skip_group_check=True)

            def x_transpose(i):
                a, e = XT_GROUPS[i]
                pe.wait_ge(x0_in if i == 0 else x_in, 16 if i == 0 else 16 * TG)
                for q in range(a, e):
                    last = nc.tensor.transpose(xT_ps[i][:, (q - a) * P:(q - a + 1) * P], x_rows[:, q, :], ident[:, :])
                last.then_inc(xT_ready, 1)

            def gate_cols(k, g):
                return lstm_ps[k % 2][:, :].rearrange("p (t w) -> p t w", t=TG)[:, :, g * N:(g + 1) * N]

            def lstm_x(k, g):
                mm(gate_cols(k, g), Wx_s[:, g * P:(g + 1) * P], X2[:, k * P:(k + 1) * P])

            def gru_x(p, j):
                a = 2 * p % 4 * N
                if j == 1:
                    dst = z_ps[p % 2][:, 0:2 * N]
                else:
                    dst = rh_ps[p % 2][:, 0:4 * N].rearrange("p (t w) -> p t w", t=2)[:, :, j // 2 * N:(j // 2 + 1) * N]
                return mm(dst, gW[:, j, :], X1[:, a:a + 2 * N])

            def zeros(bank_, cols=512):
                return nc.tensor.matmul(bank_[:, 0:cols], busy[:, :], busy[:, 0:1].to_broadcast([P, cols]),
                                        start=True, stop=True, skip_group_check=True)

            def keep_busy(n, cols=512):
                for _ in range(n):
                    zeros(idle_ps, cols)

            def open_bank(bank_):
                zeros(bank_).then_inc(opened, 1)

            pe.wait_ge(busy_zero, 1)
            open_bank(lstm_ps[0])
            open_bank(lstm_ps[1])
            keep_busy(BUSY)
            pe.wait_ge(ident_ready, 1)
            pe.wait_ge(cond_in, 16)
            nc.tensor.transpose(cond_ps[:, 0:N], cond_rows[:, :], ident[0:N, 0:N]).then_inc(condT_ps_ready, 1)
            x_transpose(0)
            keep_busy(2)
            pe.wait_ge(wx_ready, 2)
            pe.wait_ge(x2_ready, 1)
            pe.wait_ge(lstm_seeded, 1)
            for g in range(NG):
                lstm_x(0, g)
            pe.wait_ge(condT_ready, 2)
            pe.wait_ge(wh_in, 16)

            def recurrent(t, g, part, hpart):
                return mm(gate_cols(t // TG, g)[:, t % TG, :], Wh_part[:, part, g * P:(g + 1) * P],
                          H_part[:, (t - 1) % 2, hpart, :])

            def slot(t):
                k, s_ = t // TG, t % TG
                g = t - LAG
                if t == 0:
                    for gate in range(NG):
                        last = mm(gate_cols(0, gate)[:, 0, :], Wh_raw[:, gate * P:(gate + 1) * P],
                                  condT[:, :] if gate == 3 else condT_half[:, :])
                    last.then_inc(lstm_pre, 1)
                elif t < T:
                    if t == 1:
                        pe.wait_ge(wh_step, 4)
                        pe.wait_ge(wh_ready, 1)
                    pe.wait_ge(h_hi_ready, t)
                    for gate in range(NG):
                        for part in range(3):
                            recurrent(t, gate, part, 0)
                    pe.wait_ge(h_lo_ready, t)
                    for gate in range(NG):
                        for part in range(2):
                            last = recurrent(t, gate, part, 1)
                    last.then_inc(lstm_pre, 1)
                if t == 0:
                    x_transpose(1)
                    pe.wait_ge(gc_in, 48)
                    for j in range(3):
                        last = nc.tensor.matmul(cond_ps[:, 128 + j * N:128 + (j + 1) * N], gC[:, j, :], condT[:, :],
                                                start=(j == 0), stop=True, skip_group_check=True)
                    last.then_inc(v_ps_ready, 1)
                if t == 1:
                    x_transpose(2)
                if t == 0:
                    keep_busy(2)
                if t == 1:
                    pe.wait_ge(x2_ready, 2)
                    open_bank(rh_ps[0])
                    open_bank(rh_ps[1])
                    open_bank(z_ps[0])
                if t == 2:
                    pe.wait_ge(x2_ready, 3)
                    open_bank(z_ps[1])
                if g >= 0:
                    gp = (g - 1) % 4 * N
                    if g == 0:
                        pe.wait_ge(gu_ready, 1)
                    pe.wait_ge(g_ready, g + 1)
                    mm(r_cols(g), gU[:, 0, :], G[:, gp:gp + N]).then_inc(r_pre, 1)
                    mm(z_cols(g), gU[:, 1, :], G[:, gp:gp + N]).then_inc(z_pre, 1)
                if t % 2 == 0 and 2 <= t <= T:
                    p = t // 2 - 1
                    if p == 0:
                        pe.wait_ge(gw_ready, 2)
                    pe.wait_ge(gru_seeded, 2 * p + 2)
                    pe.wait_ge(x1_ready, p + 1)
                    gru_x(p, 0)
                    gru_x(p, 1)
                if s_ % 2 == 1 and k + 1 < Q:
                    if s_ == 1:
                        pe.wait_ge(lstm_seeded, k + 2)
                    lstm_x(k + 1, s_ - 1)
                    lstm_x(k + 1, s_)
                if t >= T:
                    keep_busy(1)
                if g >= 0:
                    pe.wait_ge(rh_ready, g + 1)
                    mm(hh_cols(g), gU[:, 2, :], RH[:, g % 2, :]).then_inc(hh_pre, 1)
                if t % 2 == 0 and 2 <= t <= T:
                    gru_x(t // 2 - 1, 2).then_inc(x1_used, 1)
                if s_ == 3 and t >= 7:
                    y_transpose(k - 1)
                keep_busy(1 if t < T - 1 else 2)

            def y_transpose(q):
                pe.wait_ge(y_ready, 2 * q + 2)
                if q >= 1:
                    pe.wait_ge(y_rows_ready, q)
                nc.tensor.transpose(y_ps[:, 0:P], Y[:, :], ident[:, :]).then_inc(yT_ready, 1)

            run_slots(slot)
            y_transpose(Q - 1)


_INS = ['x', 'cond_1024', 'L0_cond_Wx', 'L0_cond_Wh', 'L0_cond_b',
        'L1_cond_W_z', 'L1_cond_U_z', 'L1_cond_C_z', 'L1_cond_b_z',
        'L1_cond_W_r', 'L1_cond_U_r', 'L1_cond_C_r', 'L1_cond_b_r',
        'L1_cond_W', 'L1_cond_U', 'L1_cond_C', 'L1_cond_b']


def kernel(**inputs):
    import numpy as _np
    import concourse.bacc as _bacc
    from concourse import mybir as _mybir
    from concourse.bass_utils import run_bass_kernel_spmd as _run

    nc = _bacc.Bacc("TRN2", target_bir_lowering=False, num_devices=1)
    arrays, args = {}, []
    for name in _INS:
        a = _np.ascontiguousarray(inputs[name])
        arrays[f"in_{name}_dram"] = a
        args.append(nc.dram_tensor(f"in_{name}_dram", a.shape, _mybir.dt.from_np(a.dtype), kind="ExternalInput").ap())
    args.append(nc.dram_tensor("out_0_dram", inputs["x"].shape, _mybir.dt.float32, kind="ExternalOutput").ap())
    lstm_then_gru_residual(nc, *args)
    r = _run(nc, [arrays], core_ids=[0])
    return r.results[0]["out_0_dram"]
```

```python
import concourse.bass as bass
from concourse import mybir
from contextlib import ExitStack

F32 = mybir.dt.float32
BF16 = mybir.dt.bfloat16
F16 = mybir.dt.float16
ALU = mybir.AluOpType
ACT = mybir.ActivationFunctionType


def lstm_then_gru_residual(nc, x, cond, Wx, Wh, b, W_z, U_z, C_z, b_z, W_r, U_r, C_r, b_r, W, U, C, b_h, out):
    N, T, D = x.shape
    P = 128
    BANK = 512
    assert D == P and Wx.shape[1] == 4 * P and T == 32 and 4 * N == P
    NG = 4
    L = NG * N
    TG = P // N
    Q = T // TG
    LAG = 2
    BUSY = 4
    FILL = 320

    x_groups = x.rearrange("b (q t) d -> q t b d", t=TG)
    out_groups = out.rearrange("b (q t) d -> q t b d", t=TG)

    ctx = ExitStack()
    with ctx:
        def sb(name, shape, dt=F32):
            return ctx.enter_context(nc.sbuf_tensor(name, shape, dt))

        def bank(name):
            return ctx.enter_context(nc.psum_tensor(name, [P, BANK], F32))

        def sem(name):
            return ctx.enter_context(nc.semaphore(name))

        ident = sb("ident", [P, P])
        x_rows = sb("x_rows", [P, Q, D])
        cond_rows = sb("cond_rows", [N, D])
        X2 = sb("X2", [P, T * N])
        condT = sb("condT", [P, N])
        condT_half = sb("condT_half", [P, N])
        x_half = sb("x_half", [P, P])
        x_first = sb("x_first", [P, P])
        Wx_raw = sb("Wx_raw", [P, NG * P])
        Wh_raw = sb("Wh_raw", [P, NG * P])
        Wx_s = sb("Wx_s", [P, NG * P])
        Wh_part = sb("Wh_part", [P, 3, NG * P], BF16)
        Wh_left = sb("Wh_left", [P, NG * P])
        gW_raw = sb("gW_raw", [P, 3, P])
        gU_raw = sb("gU_raw", [P, 3, P])
        gC = sb("gC", [P, 3, P])
        gW = sb("gW", [P, 3, P])
        gU = sb("gU", [P, 3, P])
        gb = sb("gb", [P, 3])
        V_rh = sb("V_rh", [P, 2, 2, N])
        V_z = sb("V_z", [P, 2, N])
        b_cols = sb("b_cols", [P, NG])
        b_wide = sb("b_wide", [P, TG, NG, N])
        gates = sb("gates", [P, 2, 5 * N])
        vu = sb("vu", [P, 2, 2 * N])
        th = sb("th", [P, 2, N])
        H = sb("H", [P, TG * N])
        H_part = sb("H_part", [P, 2, 2, N], F16)
        X1 = sb("X1", [P, TG * N])
        G = sb("G", [P, 2 * TG * N])
        tr = sb("tr", [P, 2, N])
        tz = sb("tz", [P, 2, N])
        hh = sb("hh", [P, 2, N])
        RH = sb("RH", [P, 2, N])
        An = sb("An", [P, 2, N])
        Pz = sb("Pz", [P, 2, N])
        y_rows = sb("y_rows", [P, D])
        warm = sb("warm", [P, 1])
        busy = sb("busy", [P, 1], BF16)

        lstm_ps = [bank("lstm_ps0"), bank("lstm_ps1")]
        rh_ps = [bank("rh_ps0"), bank("rh_ps1")]
        z_ps = [bank("z_ps0"), bank("z_ps1")]
        y_ps = bank("y_ps")
        idle_ps = bank("idle_ps")
        cond_ps = y_ps
        xT_ps = [rh_ps[0], z_ps[0], z_ps[1]]
        XT_GROUPS = [(0, 1), (1, 4), (4, Q)]
        V_COLS = P

        x0_in = sem("x0_in")
        x_in = sem("x_in")
        cond_in = sem("cond_in")
        wx_in = sem("wx_in")
        wh_in = sem("wh_in")
        b_in = sem("b_in")
        gw_in = sem("gw_in")
        gu_in = sem("gu_in")
        gc_in = sem("gc_in")
        gb_in = sem("gb_in")
        ident_zero = sem("ident_zero")
        ident_ready = sem("ident_ready")
        warm_zero = sem("warm_zero")
        busy_zero = sem("busy_zero")
        opened = sem("opened")
        xT_ready = sem("xT_ready")
        x_first_ready = sem("x_first_ready")
        x2_ready = sem("x2_ready")
        condT_ps_ready = sem("condT_ps_ready")
        condT_ready = sem("condT_ready")
        first_seeded = sem("first_seeded")
        wx_ready = sem("wx_ready")
        wh_step = sem("wh_step")
        wh_left_ready = sem("wh_left_ready")
        wh_ready = sem("wh_ready")
        b_ready = sem("b_ready")
        gw_ready = sem("gw_ready")
        gu_ready = sem("gu_ready")
        v_ps_ready = sem("v_ps_ready")
        v_ready = sem("v_ready")
        c_ready = sem("c_ready")
        h_hi_ready = sem("h_hi_ready")
        h_ready = sem("h_ready")
        h_lo_ready = sem("h_lo_ready")
        g_ready = sem("g_ready")
        lstm_pre = sem("lstm_pre")
        gates_ready = sem("gates_ready")
        vu_ready = sem("vu_ready")
        th_ready = sem("th_ready")
        r_pre = sem("r_pre")
        z_pre = sem("z_pre")
        r_ready = sem("r_ready")
        z_ready = sem("z_ready")
        rh_ready = sem("rh_ready")
        hh_pre = sem("hh_pre")
        hh_ready = sem("hh_ready")
        pz_ready = sem("pz_ready")
        gru_seeded = sem("gru_seeded")
        x1_ready = sem("x1_ready")
        lstm_seeded = sem("lstm_seeded")
        yx_done = sem("yx_done")
        yT_ready = sem("yT_ready")
        y_rows_ready = sem("y_rows_ready")
        out_done = sem("out_done")

        block = ctx.enter_context(nc.Block())

        def gate_cols(k, g):
            return lstm_ps[k % 2][:, :].rearrange("p (t w) -> p t w", t=TG)[:, :, g * N:(g + 1) * N]

        def r_cols(g):
            return rh_ps[g // 2 % 2][:, g % 2 * 2 * N:g % 2 * 2 * N + N]

        def hh_cols(g):
            return rh_ps[g // 2 % 2][:, g % 2 * 2 * N + N:g % 2 * 2 * N + 2 * N]

        def z_cols(g):
            return z_ps[g // 2 % 2][:, g % 2 * N:g % 2 * N + N]

        def g_cols(g):
            c = g % (2 * TG) * N
            return G[:, c:c + N]

        def b_over_group(g):
            return b_cols[:, g:g + 1].rearrange("p (a b) -> p a b", a=1).to_broadcast([P, TG, N])

        def gate_scale(g):
            return 0.5 if g < 3 else 1.0

        def run_slots(slot):
            for t in range(T + LAG):
                slot(t)

        @block.sync
        def _(sp):
            sp.dma_start(x_rows[:, 0, :], x_groups[0]).then_inc(x0_in, 16)
            sp.dma_start(Wx_raw[:, :], Wx).then_inc(wx_in, 16)
            sp.dma_start(Wh_raw[:, :], Wh).then_inc(wh_in, 16)
            for j in range(TG):
                sp.dma_start(x_rows[j * N:(j + 1) * N, 1:Q, :],
                             x.rearrange("b (q t) d -> t b q d", t=TG)[j, :, 1:Q, :]).then_inc(x_in, 16)
            for j, w in enumerate((C_r, C_z, C)):
                sp.dma_start(gC[:, j, :], w).then_inc(gc_in, 16)
            for j, w in enumerate((b_r, b_z, b_h)):
                sp.dma_start(gb[:, j:j + 1], w.rearrange("(d a) -> d a", a=1)).then_inc(gb_in, 16)
            for j, w in enumerate((W_r, W_z, W)):
                sp.dma_start(gW_raw[:, j, :], w).then_inc(gw_in, 16)

            with sp.Fori(0, Q - 1) as q:
                sp.wait_ge(y_rows_ready, q + 1)
                sp.dma_start(out_groups[bass.ds(q, 1)], y_rows[:, :]).then_inc(out_done, 16)
            sp.wait_ge(y_rows_ready, Q)
            sp.dma_start(out_groups[Q - 1], y_rows[:, :]).then_inc(out_done, 16)
            sp.wait_ge(out_done, 16 * Q)

        @block.gpsimd
        def _(pool):
            nc.gpsimd.memset(ident[:, :], 0.0).then_inc(ident_zero, 1)
            pool.wait_ge(ident_zero, 1)
            nc.gpsimd.affine_select(out=ident[:, :], in_=ident[:, :], compare_op=ALU.not_equal, fill=1.0,
                                    base=0, pattern=[[-1, P]], channel_multiplier=1).then_inc(ident_ready, 1)
            for j, w in enumerate((U_r, U_z, U)):
                pool.dma_start(gU_raw[:, j, :], w).then_inc(gu_in, 16)
            pool.wait_ge(b_in, 16)
            for g in range(NG):
                nc.gpsimd.tensor_scalar(b_wide[:, :, g, :], b_over_group(g), gate_scale(g), None,
                                        ALU.mult).then_inc(b_ready, 1)
            pool.wait_ge(wh_step, 4)
            nc.gpsimd.tensor_tensor(Wh_part[:, 2, 2 * P:], Wh_left[:, 2 * P:], Wh_part[:, 1, 2 * P:],
                                    ALU.subtract).then_inc(wh_ready, 1)

            def slot(t):
                if t % 2 == 0 and 2 <= t <= T:
                    p = t // 2 - 1
                    pool.wait_ge(h_ready, 2 * p + 2)
                    for i, (first, _) in enumerate(XT_GROUPS):
                        if p == first * TG // 2:
                            pool.wait_ge(x2_ready, i + 1)
                    if p >= 2:
                        pool.wait_ge(hh_pre, 2 * p - 3)
                        pool.wait_ge(yx_done, p // 2)
                    c = 2 * p % TG * N
                    nc.gpsimd.tensor_tensor(X1[:, c:c + 2 * N], X2[:, p * 2 * N:(p + 1) * 2 * N],
                                            H[:, c:c + 2 * N], ALU.add).then_inc(x1_ready, 1)

            run_slots(slot)

        @block.scalar
        def _(act):
            act.dma_start(b_cols[:, :], b.rearrange("(g d) -> d g", g=NG),
                          allow_slow_non_contiguous=True).then_inc(b_in, 16)
            act.dma_start(cond_rows[:, :], cond).then_inc(cond_in, 16)
            act.wait_ge(warm_zero, 1)
            nc.scalar.activation(warm[:, :], warm[:, :], ACT.Tanh)

            def seed_lstm(k):
                nc.scalar.copy(lstm_ps[k % 2][:, :], b_wide[:, :, :, :].rearrange("p t g n -> p (t g n)")
                               ).then_inc(lstm_seeded, 1)

            def seed_gru(p):
                nc.scalar.copy(rh_ps[p % 2][:, 0:4 * N], V_rh[:, :, :, :].rearrange("p t g n -> p (t g n)")
                               ).then_inc(gru_seeded, 1)
                nc.scalar.copy(z_ps[p % 2][:, 0:2 * N], V_z[:, :, :].rearrange("p t n -> p (t n)")
                               ).then_inc(gru_seeded, 1)

            act.wait_ge(xT_ready, 1)
            nc.scalar.mul(x_half[:, :], xT_ps[0][:, 0:P], 0.5).then_inc(x_first_ready, 1)
            nc.scalar.copy(x_first[:, :], xT_ps[0][:, 0:P]).then_inc(x_first_ready, 1)
            act.wait_ge(condT_ps_ready, 1)
            nc.scalar.mul(condT_half[:, :], cond_ps[:, 0:N], 0.5).then_inc(condT_ready, 1)
            nc.scalar.copy(condT[:, :], cond_ps[:, 0:N]).then_inc(condT_ready, 1)

            def x2_copy(i):
                a, e = XT_GROUPS[i]
                act.wait_ge(xT_ready, i + 1)
                nc.scalar.mul(X2[:, a * P:e * P], xT_ps[i][:, 0:(e - a) * P], 2.0).then_inc(x2_ready, 1)

            act.wait_ge(wh_left_ready, 1)
            nc.scalar.copy(Wh_part[:, 1, 0:3 * P], Wh_left[:, 0:3 * P]).then_inc(wh_step, 1)
            act.wait_ge(wh_left_ready, 2)
            nc.scalar.copy(Wh_part[:, 1, 3 * P:], Wh_left[:, 3 * P:]).then_inc(wh_step, 1)

            def slot(t):
                g = t - LAG
                if t < T:
                    act.wait_ge(lstm_pre, t + 1)
                    nc.scalar.activation(gates[:, t % 2, 0:L], lstm_ps[t // TG % 2][:, t % TG * L:(t % TG + 1) * L],
                                         ACT.Tanh).then_inc(gates_ready, 1)
                if g >= 1:
                    act.wait_ge(r_pre, g)
                    nc.scalar.activation(tr[:, g % 2, :], r_cols(g), ACT.Tanh).then_inc(r_ready, 1)
                if t < T:
                    act.wait_ge(c_ready, t + 2)
                    nc.scalar.activation(th[:, t % 2, :], gates[:, (t + 1) % 2, L:L + N], ACT.Tanh,
                                         scale=0.5).then_inc(th_ready, 1)
                if g >= 0:
                    act.wait_ge(z_pre, g + 1)
                    nc.scalar.activation(tz[:, g % 2, :], z_cols(g), ACT.Tanh).then_inc(z_ready, 1)
                    act.wait_ge(hh_pre, g + 1)
                    nc.scalar.activation(hh[:, g % 2, :], hh_cols(g), ACT.Tanh).then_inc(hh_ready, 1)
                if t == 0:
                    x2_copy(0)
                    x2_copy(1)
                    act.wait_ge(b_ready, NG)
                    act.wait_ge(opened, 2)
                    seed_lstm(1)
                if t == 1:
                    x2_copy(2)
                    act.wait_ge(v_ready, 3)
                    act.wait_ge(opened, 5)
                    seed_gru(0)
                if t == 2:
                    act.wait_ge(opened, 6)
                if t % 2 == 0 and 2 <= t < T:
                    if t >= 4:
                        act.wait_ge(hh_ready, t - 2)
                    seed_gru(t // 2)
                if t % TG == TG - 1 and t // TG + 2 < Q:
                    act.wait_ge(gates_ready, t + 1)
                    seed_lstm(t // TG + 2)

            run_slots(slot)

        @block.vector
        def _(dve):
            def stt(out_, in0, scalar, in1, op0, op1):
                return nc.vector.scalar_tensor_tensor(out=out_, in0=in0, scalar=scalar, in1=in1, op0=op0, op1=op1)

            nc.vector.memset(busy[:, :], 0.0).then_inc(busy_zero, 1)
            nc.vector.memset(warm[:, :], 0.0).then_inc(warm_zero, 1)
            nc.vector.memset(gates[:, 0, L:L + N], 0.0).then_inc(c_ready, 1)
            nc.vector.memset(g_cols(-1), 0.0).then_inc(g_ready, 1)

            dve.wait_ge(b_in, 16)
            dve.wait_ge(opened, 1)
            for g in range(NG):
                nc.vector.tensor_scalar(gate_cols(0, g), b_over_group(g), gate_scale(g), None,
                                        ALU.mult).then_inc(first_seeded, 1)

            SCALED = ((0, 3 * P, 0.25), (3 * P, 4 * P, 0.5))
            dve.wait_ge(wx_in, 16)
            for c, e, scale in SCALED:
                nc.vector.tensor_scalar(Wx_s[:, c:e], Wx_raw[:, c:e], scale, None, ALU.mult).then_inc(wx_ready, 1)
            dve.wait_ge(c_ready, 1)
            dve.wait_ge(g_ready, 1)
            dve.wait_ge(wh_in, 16)
            for c, e, scale in SCALED:
                nc.vector.tensor_scalar(Wh_part[:, 0, c:e], Wh_raw[:, c:e], scale, None, ALU.mult).then_inc(wh_step, 1)
            for j, (c, e, scale) in enumerate(SCALED):
                dve.wait_ge(wh_step, j + 1)
                stt(Wh_left[:, c:e], Wh_raw[:, c:e], scale, Wh_part[:, 0, c:e],
                    ALU.mult, ALU.subtract).then_inc(wh_left_ready, 1)

            def v_setup():
                dve.wait_ge(gb_in, 48)
                dve.wait_ge(v_ps_ready, 1)
                for g, dst in enumerate((V_rh[:, :, 0, :], V_z[:, :, :], V_rh[:, :, 1, :])):
                    nc.vector.tensor_scalar(dst, cond_ps[:, V_COLS + g * N:V_COLS + (g + 1) * N]
                                            .rearrange("p (a n) -> p a n", a=1).to_broadcast([P, 2, N]),
                                            gb[:, g:g + 1], 0.5 if g < 2 else 1.0,
                                            ALU.add, ALU.mult).then_inc(v_ready, 1)

            def slot(t):
                g = t - LAG
                b_, gb_ = t % 2, g % 2
                hc = t % TG * N
                if t < T:
                    dve.wait_ge(gates_ready, t + 1)
                    stt(vu[:, b_, :], gates[:, b_, 0:2 * N], 1.0, gates[:, b_, 3 * N:5 * N],
                        ALU.add, ALU.mult).then_inc(vu_ready, 1)
                    dve.wait_ge(vu_ready, t + 1)
                    stt(gates[:, 1 - b_, L:L + N], vu[:, b_, N:2 * N], 0.5, vu[:, b_, 0:N],
                        ALU.mult, ALU.add).then_inc(c_ready, 1)
                if g >= 1:
                    dve.wait_ge(r_ready, g)
                    stt(RH[:, gb_, :], tr[:, gb_, :], 1.0, g_cols(g - 1), ALU.add, ALU.mult).then_inc(rh_ready, 1)
                if t == 0:
                    dve.wait_ge(wh_step, 4)
                    nc.vector.tensor_tensor(Wh_part[:, 2, 0:2 * P], Wh_left[:, 0:2 * P], Wh_part[:, 1, 0:2 * P],
                                            ALU.subtract).then_inc(wh_ready, 1)
                if t < T:
                    dve.wait_ge(th_ready, t + 1)
                    stt(H_part[:, b_, 0, :], gates[:, b_, 2 * N:3 * N], 1.0, th[:, b_, :],
                        ALU.add, ALU.mult).then_inc(h_hi_ready, 1)
                    stt(H[:, hc:hc + N], gates[:, b_, 2 * N:3 * N], 1.0, th[:, b_, :],
                        ALU.add, ALU.mult).then_inc(h_ready, 1)
                if g >= 0:
                    dve.wait_ge(z_ready, g + 1)
                    stt(An[:, gb_, :], tz[:, gb_, :], -1.0, g_cols(g - 1), ALU.add, ALU.mult)
                if t < T - 1:
                    dve.wait_ge(h_ready, t + 1)
                    nc.vector.tensor_tensor(H_part[:, b_, 1, :], H[:, hc:hc + N], H_part[:, b_, 0, :],
                                            ALU.subtract).then_inc(h_lo_ready, 1)
                if g >= 0:
                    dve.wait_ge(hh_ready, g + 1)
                    stt(Pz[:, gb_, :], tz[:, gb_, :], 1.0, hh[:, gb_, :], ALU.add, ALU.mult).then_inc(pz_ready, 1)
                    dve.wait_ge(pz_ready, g + 1)
                    stt(g_cols(g), An[:, gb_, :], -0.5, Pz[:, gb_, :], ALU.mult, ALU.add).then_inc(g_ready, 1)
                if t == 0:
                    v_setup()
                if t == 1:
                    dve.wait_ge(gw_in, 48)
                    nc.vector.tensor_scalar(gW[:, 0:2, :], gW_raw[:, 0:2, :], 0.25, None, ALU.mult).then_inc(gw_ready, 1)
                    nc.vector.tensor_scalar(gW[:, 2, :], gW_raw[:, 2, :], 0.5, None, ALU.mult).then_inc(gw_ready, 1)
                    dve.wait_ge(gu_in, 48)
                    nc.vector.tensor_scalar(gU[:, :, :], gU_raw[:, :, :], 0.25, None, ALU.mult).then_inc(gu_ready, 1)
                if t % TG == TG - 1 and t > TG:
                    y_out(t // TG - 1)

            def y_out(q):
                dve.wait_ge(yT_ready, q + 1)
                if q >= 1:
                    dve.wait_ge(out_done, 16 * q)
                nc.vector.tensor_scalar(y_rows[:, :], y_ps[:, 0:P], 0.5, None, ALU.mult).then_inc(y_rows_ready, 1)

            run_slots(slot)
            y_out(Q - 1)

        @block.tensor
        def _(pe):
            def mm(out_, lhsT, rhs):
                return nc.tensor.matmul(out_, lhsT, rhs, start=False, stop=False, skip_group_check=True)

            def x_transpose(i):
                a, e = XT_GROUPS[i]
                pe.wait_ge(x0_in if i == 0 else x_in, 16 if i == 0 else 16 * TG)
                for q in range(a, e):
                    last = nc.tensor.transpose(xT_ps[i][:, (q - a) * P:(q - a + 1) * P], x_rows[:, q, :], ident[:, :])
                last.then_inc(xT_ready, 1)

            def lstm_x(k, g):
                mm(gate_cols(k, g), Wx_s[:, g * P:(g + 1) * P], X2[:, k * P:(k + 1) * P])

            def gru_x(p, j):
                a = 2 * p % TG * N
                if j == 1:
                    dst = z_ps[p % 2][:, 0:2 * N]
                else:
                    dst = rh_ps[p % 2][:, 0:4 * N].rearrange("p (t w) -> p t w", t=2)[:, :, j // 2 * N:(j // 2 + 1) * N]
                return mm(dst, gW[:, j, :], X1[:, a:a + 2 * N])

            def zeros(bank_, cols=BANK):
                return nc.tensor.matmul(bank_[:, 0:cols], busy[:, :].to_broadcast([P, P]),
                                        busy[:, :].to_broadcast([P, cols]),
                                        start=True, stop=True, skip_group_check=True)

            def keep_busy(n, cols=BANK):
                for _ in range(n):
                    zeros(idle_ps, cols)

            def open_bank(bank_, cols=BANK):
                zeros(bank_, cols).then_inc(opened, 1)

            pe.wait_ge(busy_zero, 1)
            open_bank(lstm_ps[0])
            open_bank(lstm_ps[1])
            keep_busy(BUSY)
            pe.wait_ge(ident_ready, 1)
            x_transpose(0)
            keep_busy(2)
            pe.wait_ge(cond_in, 16)
            nc.tensor.transpose(cond_ps[:, 0:N], cond_rows[:, :], ident[0:N, 0:N]).then_inc(condT_ps_ready, 1)
            pe.wait_ge(first_seeded, NG)
            pe.wait_ge(wx_in, 16)
            pe.wait_ge(x_first_ready, 2)
            for g in range(NG):
                mm(gate_cols(0, g), Wx_raw[:, g * P:(g + 1) * P], x_half[:, :] if g < 3 else x_first[:, :])
            pe.wait_ge(condT_ready, 2)
            pe.wait_ge(wh_in, 16)

            def recurrent(t, g, part, hpart):
                return mm(gate_cols(t // TG, g)[:, t % TG, :], Wh_part[:, part, g * P:(g + 1) * P],
                          H_part[:, (t - 1) % 2, hpart, :])

            def slot(t):
                k, s_ = t // TG, t % TG
                g = t - LAG
                if t == 0:
                    for gate in range(NG):
                        last = mm(gate_cols(0, gate)[:, 0, :], Wh_raw[:, gate * P:(gate + 1) * P],
                                  condT[:, :] if gate == 3 else condT_half[:, :])
                    last.then_inc(lstm_pre, 1)
                elif t < T:
                    if t == 1:
                        pe.wait_ge(wh_step, 4)
                        pe.wait_ge(wh_ready, 2)
                    pe.wait_ge(h_hi_ready, t)
                    for gate in range(NG):
                        for part in range(3):
                            recurrent(t, gate, part, 0)
                    pe.wait_ge(h_lo_ready, t)
                    for gate in range(NG):
                        for part in range(2):
                            last = recurrent(t, gate, part, 1)
                    last.then_inc(lstm_pre, 1)
                if t == 0:
                    x_transpose(1)
                    pe.wait_ge(gc_in, 48)
                    for j in range(3):
                        last = nc.tensor.matmul(cond_ps[:, V_COLS + j * N:V_COLS + (j + 1) * N], gC[:, j, :], condT[:, :],
                                                start=(j == 0), stop=True, skip_group_check=True)
                    last.then_inc(v_ps_ready, 1)
                    keep_busy(1)
                if t == 1:
                    x_transpose(2)
                    pe.wait_ge(x2_ready, 2)
                    open_bank(rh_ps[0], 4 * N)
                    open_bank(rh_ps[1], 4 * N)
                    open_bank(z_ps[0], 2 * N)
                if t == 2:
                    pe.wait_ge(x2_ready, 3)
                    open_bank(z_ps[1], 2 * N)
                if g >= 0 and g % 2 == 0:
                    p = g // 2
                    if p == 0:
                        pe.wait_ge(gw_ready, 2)
                    pe.wait_ge(gru_seeded, 2 * p + 2)
                    pe.wait_ge(x1_ready, p + 1)
                    gru_x(p, 0)
                if s_ == 1 and t > TG:
                    y_x1(k - 1)
                if s_ == 3:
                    if k + 1 < Q:
                        lstm_x(k + 1, 2)
                    elif t < T:
                        keep_busy(1)
                if g == 0:
                    gru_x(0, 1).then_inc(z_pre, 1)
                    gru_x(0, 2).then_inc(hh_pre, 1)
                if g >= 1:
                    if g == 1:
                        pe.wait_ge(gu_ready, 1)
                    pe.wait_ge(g_ready, g + 1)
                    mm(r_cols(g), gU[:, 0, :], g_cols(g - 1)).then_inc(r_pre, 1)
                    if g % 2 == 0:
                        gru_x(g // 2, 1)
                    mm(z_cols(g), gU[:, 1, :], g_cols(g - 1)).then_inc(z_pre, 1)
                if g >= 2 and g % 2 == 0:
                    pe.wait_ge(r_ready, g)
                    gru_x(g // 2, 2)
                if s_ == 1 and k + 1 < Q:
                    if k == 0:
                        pe.wait_ge(wx_ready, 2)
                    pe.wait_ge(lstm_seeded, k + 1)
                    lstm_x(k + 1, 0)
                    lstm_x(k + 1, 1)
                if s_ == 3:
                    if t > TG:
                        y_g(k - 1)
                    if k + 1 < Q:
                        lstm_x(k + 1, 3)
                if t >= T or k + 1 == Q and s_ % 2 == 1:
                    keep_busy(1)
                if g >= 1:
                    pe.wait_ge(rh_ready, g)
                    mm(hh_cols(g), gU[:, 2, :], RH[:, g % 2, :]).then_inc(hh_pre, 1)
                if 2 <= t < T - 1:
                    keep_busy(1, FILL)
                if t >= T - 1:
                    keep_busy(2)

            def y_x1(q):
                if q >= 1:
                    pe.wait_ge(y_rows_ready, q)
                nc.tensor.matmul(y_ps[:, 0:P], X1[:, :], ident[:, :], start=True, stop=False,
                                 skip_group_check=True).then_inc(yx_done, 1)

            def y_g(q):
                gc = q % 2 * TG * N
                pe.wait_ge(g_ready, TG * q + TG + 1)
                mm(y_ps[:, 0:P], G[:, gc:gc + TG * N], ident[:, :]).then_inc(yT_ready, 1)

            run_slots(slot)
            y_g(Q - 1)


_INS = ['x', 'cond_1024', 'L0_cond_Wx', 'L0_cond_Wh', 'L0_cond_b',
        'L1_cond_W_z', 'L1_cond_U_z', 'L1_cond_C_z', 'L1_cond_b_z',
        'L1_cond_W_r', 'L1_cond_U_r', 'L1_cond_C_r', 'L1_cond_b_r',
        'L1_cond_W', 'L1_cond_U', 'L1_cond_C', 'L1_cond_b']


def kernel(**inputs):
    import numpy as _np
    import concourse.bacc as _bacc
    from concourse import mybir as _mybir
    from concourse.bass_utils import run_bass_kernel_spmd as _run

    nc = _bacc.Bacc("TRN2", target_bir_lowering=False, num_devices=1)
    arrays, args = {}, []
    for name in _INS:
        a = _np.ascontiguousarray(inputs[name])
        arrays[f"in_{name}_dram"] = a
        args.append(nc.dram_tensor(f"in_{name}_dram", a.shape, _mybir.dt.from_np(a.dtype), kind="ExternalInput").ap())
    args.append(nc.dram_tensor("out_0_dram", inputs["x"].shape, _mybir.dt.float32, kind="ExternalOutput").ap())
    lstm_then_gru_residual(nc, *args)
    r = _run(nc, [arrays], core_ids=[0])
    return r.results[0]["out_0_dram"]
```
